# Optimizing a Trainium2 kernel written in Bass

```python
import numpy as np
import jax
import jax.numpy as jnp

def _softmax(x, axis=-1):
    return jax.nn.softmax(x, axis=axis)

def _gelu(x):
    return jax.nn.gelu(x, approximate=True)

def _silu(x):
    return jax.nn.silu(x)

def _sigmoid(x):
    return jax.nn.sigmoid(x)

def _layernorm(x, axis=-1, eps=1e-05):
    m = jnp.mean(x, axis=axis, keepdims=True)
    v = jnp.var(x, axis=axis, keepdims=True)
    return (x - m) / jnp.sqrt(v + eps)

def _scatter_add(tgt, idx, src, axis=0):
    return tgt.at[idx].add(src)

def _segment_sum(src, seg, n):
    return jax.ops.segment_sum(src, seg, n)
kernel_name = 'mk_gnn_resnorm_d4_gnn_r32_152497'

def setup_inputs(seed: int=0):
    np.random.seed(seed)
    _w = jnp.asarray

    def _rec_inputs():
        import jax
        import jax.numpy as jnp
        _gk = jax.random.key(seed)
        x = -0.000202 + 1 * jax.random.normal(jax.random.fold_in(_gk, 1), (3125, 128), jnp.float32)
        src = jax.random.randint(jax.random.fold_in(_gk, 2), (50000,), 0, 3125, jnp.int32)
        dst = jax.random.randint(jax.random.fold_in(_gk, 3), (50000,), 0, 3125, jnp.int32)
        _o = jnp.argsort(dst, stable=True)
        src = src[_o]
        dst = dst[_o]
        edge_type_4 = jax.random.randint(jax.random.fold_in(_gk, 13), (50000,), 0, 4, jnp.int32)
        edge_weight = jax.random.uniform(jax.random.fold_in(_gk, 14), (50000,), jnp.float32, 0.0, 0.999996)
        return (x, src, dst, edge_type_4, edge_weight)
    x, src, dst, edge_type_4, edge_weight = _rec_inputs()

    def _L0_gnn_setup():
        import jax, jax.numpy as jnp
        import numpy as np
        key = jax.random.key(seed)
        k1, k2, k3 = jax.random.split(key, 3)
        N, E, D = (50000, 18750, 128)
        x = jax.random.normal(k1, (N, D), dtype=jnp.float32)
        src = jax.random.randint(k2, (E,), 0, N, dtype=jnp.int64)
        dst = jax.random.randint(k3, (E,), 0, N, dtype=jnp.int64)
        return {'x': x, 'src': src, 'dst': dst}
    _L0_gnn_all = _L0_gnn_setup()
    _L0_gnn_in = {k: v for k, v in _L0_gnn_all.items() if k in ()}
    del _L0_gnn_all

    def _L1_gnn_setup():
        import jax, jax.numpy as jnp
        import numpy as np
        N_NODES = 50000
        N_EDGES = 18750
        D_IN = 128
        D_OUT = 128
        BN_EPS = 1e-05

        def batchnorm(h, gamma, beta):
            mean = jnp.mean(h, axis=0)
            var = jnp.var(h, axis=0)
            return (h - mean) * jax.lax.rsqrt(var + BN_EPS) * gamma + beta
        key = jax.random.key(seed)
        ks = jax.random.split(key, 6)
        x = jax.random.normal(ks[0], (N_NODES, D_IN), dtype=jnp.float32)
        edge_index = jax.random.randint(ks[1], (2, N_EDGES), 0, N_NODES, dtype=jnp.int64)
        s_in = 1.0 / np.sqrt(D_IN)
        s_out = 1.0 / np.sqrt(D_OUT)
        return {'x': x, 'edge_index': edge_index, 'W_mlp': jax.random.normal(ks[2], (D_IN, D_OUT), dtype=jnp.float32) * s_in, 'b_mlp': jax.random.normal(ks[3], (D_OUT,), dtype=jnp.float32) * s_in, 'gamma1': jnp.ones((D_OUT,), dtype=jnp.float32), 'beta1': jnp.zeros((D_OUT,), dtype=jnp.float32), 'W_conv': jax.random.normal(ks[4], (D_OUT, D_OUT), dtype=jnp.float32) * s_out, 'b_conv': jax.random.normal(ks[5], (D_OUT,), dtype=jnp.float32) * s_out, 'gamma2': jnp.ones((D_OUT,), dtype=jnp.float32), 'beta2': jnp.zeros((D_OUT,), dtype=jnp.float32)}
    _L1_gnn_all = _L1_gnn_setup()
    _L1_gnn_in = {k: v for k, v in _L1_gnn_all.items() if k in ('W_mlp', 'b_mlp', 'gamma1', 'beta1', 'W_conv', 'b_conv', 'gamma2', 'beta2')}
    del _L1_gnn_all

    def _L2_gnn_setup():
        import jax, jax.numpy as jnp
        import numpy as np
        N_NODES = 50000
        N_EDGES = 25000
        HIDDEN = 128
        HEADS = 4
        LAYERS = 2
        NEG_SLOPE = 0.2

        def _gat_layer(x, src, dst, W, a_s, a_d, b):
            N = x.shape[0]
            h = (x @ W).reshape(N, HEADS, HIDDEN)
            alpha_src = jnp.einsum('nhc,hc->nh', h, a_s)
            alpha_dst = jnp.einsum('nhc,hc->nh', h, a_d)
            alpha = alpha_src[src] + alpha_dst[dst]
            alpha = jnp.where(alpha >= 0, alpha, NEG_SLOPE * alpha)
            amax = jax.ops.segment_max(alpha, dst, num_segments=N)
            ex = jnp.exp(alpha - amax[dst])
            denom = jax.ops.segment_sum(ex, dst, num_segments=N)
            w = ex / (denom[dst] + 1e-16)
            msg = h[src] * w[:, :, None]
            out = jax.ops.segment_sum(msg, dst, num_segments=N)
            return out.mean(axis=1) + b
        key = jax.random.key(seed)
        ks = jax.random.split(key, 12)
        s_in = 1.0 / np.sqrt(HIDDEN)
        x = jax.random.normal(ks[0], (N_NODES, HIDDEN), dtype=jnp.float32)
        edge_index = jax.random.randint(ks[1], (2, N_EDGES), 0, N_NODES, dtype=jnp.int64)
        conv_w = jax.random.normal(ks[2], (LAYERS, HIDDEN, HEADS * HIDDEN), dtype=jnp.float32) * s_in
        att_src = jax.random.normal(ks[3], (LAYERS, HEADS, HIDDEN), dtype=jnp.float32) * s_in
        att_dst = jax.random.normal(ks[4], (LAYERS, HEADS, HIDDEN), dtype=jnp.float32) * s_in
        conv_b = jax.random.normal(ks[5], (LAYERS, HIDDEN), dtype=jnp.float32) * 0.01
        proj_w = jax.random.normal(ks[6], (LAYERS, HIDDEN, HIDDEN), dtype=jnp.float32) * s_in
        proj_b = jax.random.normal(ks[7], (LAYERS, HIDDEN), dtype=jnp.float32) * 0.01
        skip_w = jax.random.normal(ks[8], (LAYERS, HIDDEN, HIDDEN), dtype=jnp.float32) * s_in
        skip_b = jax.random.normal(ks[9], (LAYERS, HIDDEN), dtype=jnp.float32) * 0.01
        return {'x': x, 'edge_index': edge_index, 'conv_w': conv_w, 'att_src': att_src, 'att_dst': att_dst, 'conv_b': conv_b, 'proj_w': proj_w, 'proj_b': proj_b, 'skip_w': skip_w, 'skip_b': skip_b}
    _L2_gnn_all = _L2_gnn_setup()
    _L2_gnn_in = {k: v for k, v in _L2_gnn_all.items() if k in ('conv_w', 'att_src', 'att_dst', 'conv_b', 'proj_w', 'proj_b', 'skip_w', 'skip_b')}
    del _L2_gnn_all

    def _L3_gnn_setup():
        import jax, jax.numpy as jnp
        import numpy as np
        NUM_RELATIONS = 4
        N_NODES = 625
        N_EDGES = 10000
        F_IN = 128
        HID = 128
        EMB = 128

        def _rgcn_conv(x, src, dst, edge_type, edge_weight, W, root, bias):
            xj = x[src]
            m = jnp.zeros((xj.shape[0], W.shape[2]), dtype=x.dtype)
            for r in range(W.shape[0]):
                mask = (edge_type == r).astype(x.dtype)[:, None]
                m = m + mask * (xj @ W[r])
            m = m * edge_weight[:, None]
            out = jax.ops.segment_sum(m, dst, num_segments=x.shape[0])
            return out + x @ root + bias
        key = jax.random.key(seed)
        ks = jax.random.split(key, 10)
        return {'x': jax.random.normal(ks[0], (N_NODES, F_IN), dtype=jnp.float32), 'edge_index': jax.random.randint(ks[1], (2, N_EDGES), 0, N_NODES, dtype=jnp.int64 if jax.config.jax_enable_x64 else jnp.int32).astype(jnp.int32), 'edge_type': jax.random.randint(ks[2], (N_EDGES,), 0, NUM_RELATIONS).astype(jnp.int32), 'edge_weight': jax.random.uniform(ks[3], (N_EDGES,), dtype=jnp.float32), 'W1': jax.random.normal(ks[4], (NUM_RELATIONS, F_IN, HID), dtype=jnp.float32) * 0.05, 'root1': jax.random.normal(ks[5], (F_IN, HID), dtype=jnp.float32) * 0.05, 'b1': jax.random.normal(ks[6], (HID,), dtype=jnp.float32) * 0.05, 'W2': jax.random.normal(ks[7], (NUM_RELATIONS, HID, EMB), dtype=jnp.float32) * 0.05, 'root2': jax.random.normal(ks[8], (HID, EMB), dtype=jnp.float32) * 0.05, 'b2': jax.random.normal(ks[9], (EMB,), dtype=jnp.float32) * 0.05}
    _L3_gnn_all = _L3_gnn_setup()
    _L3_gnn_in = {k: v for k, v in _L3_gnn_all.items() if k in ('W1', 'root1', 'b1', 'W2', 'root2', 'b2')}
    del _L3_gnn_all
    return {'x': x, 'src': src, 'dst': dst, 'edge_type_4': edge_type_4, 'edge_weight': edge_weight, 'L1_gnn_W_mlp': _L1_gnn_in['W_mlp'], 'L1_gnn_b_mlp': _L1_gnn_in['b_mlp'], 'L1_gnn_gamma1': _L1_gnn_in['gamma1'], 'L1_gnn_beta1': _L1_gnn_in['beta1'], 'L1_gnn_W_conv': _L1_gnn_in['W_conv'], 'L1_gnn_b_conv': _L1_gnn_in['b_conv'], 'L1_gnn_gamma2': _L1_gnn_in['gamma2'], 'L1_gnn_beta2': _L1_gnn_in['beta2'], 'L2_gnn_conv_w': _L2_gnn_in['conv_w'], 'L2_gnn_att_src': _L2_gnn_in['att_src'], 'L2_gnn_att_dst': _L2_gnn_in['att_dst'], 'L2_gnn_conv_b': _L2_gnn_in['conv_b'], 'L2_gnn_proj_w': _L2_gnn_in['proj_w'], 'L2_gnn_proj_b': _L2_gnn_in['proj_b'], 'L2_gnn_skip_w': _L2_gnn_in['skip_w'], 'L2_gnn_skip_b': _L2_gnn_in['skip_b'], 'L3_gnn_W1': _L3_gnn_in['W1'], 'L3_gnn_root1': _L3_gnn_in['root1'], 'L3_gnn_b1': _L3_gnn_in['b1'], 'L3_gnn_W2': _L3_gnn_in['W2'], 'L3_gnn_root2': _L3_gnn_in['root2'], 'L3_gnn_b2': _L3_gnn_in['b2']}

def reference(x, src, dst, edge_type_4, edge_weight, L1_gnn_W_mlp, L1_gnn_b_mlp, L1_gnn_gamma1, L1_gnn_beta1, L1_gnn_W_conv, L1_gnn_b_conv, L1_gnn_gamma2, L1_gnn_beta2, L2_gnn_conv_w, L2_gnn_att_src, L2_gnn_att_dst, L2_gnn_conv_b, L2_gnn_proj_w, L2_gnn_proj_b, L2_gnn_skip_w, L2_gnn_skip_b, L3_gnn_W1, L3_gnn_root1, L3_gnn_b1, L3_gnn_W2, L3_gnn_root2, L3_gnn_b2):
    import jax
    import jax.numpy as jnp

    def _L0_gnn_ref(x, src, dst):
        import jax, jax.numpy as jnp
        import numpy as np
        N = x.shape[0]
        loop = jnp.arange(N, dtype=src.dtype)
        s = jnp.concatenate([src, loop])
        d = jnp.concatenate([dst, loop])
        ones = jnp.ones(s.shape[0], dtype=x.dtype)
        in_deg = jax.ops.segment_sum(ones, d, num_segments=N)
        out_deg = jax.ops.segment_sum(ones, s, num_segments=N)
        norm_in = jnp.clip(in_deg, 1.0) ** (-0.5)
        norm_out = jnp.clip(out_deg, 1.0) ** (-0.5)
        xs = x * norm_in[:, None]
        h = jax.ops.segment_sum(xs[s], d, num_segments=N)
        return h * norm_out[:, None]

    def _L1_gnn_ref(x, edge_index, W_mlp, b_mlp, gamma1, beta1, W_conv, b_conv, gamma2, beta2):
        import jax, jax.numpy as jnp
        import numpy as np
        N_NODES = 50000
        N_EDGES = 18750
        D_IN = 128
        D_OUT = 128
        BN_EPS = 1e-05

        def batchnorm(h, gamma, beta):
            mean = jnp.mean(h, axis=0)
            var = jnp.var(h, axis=0)
            return (h - mean) * jax.lax.rsqrt(var + BN_EPS) * gamma + beta
        N = x.shape[0]
        h = x @ W_mlp + b_mlp
        h = jax.nn.relu(batchnorm(h, gamma1, beta1))
        loops = jnp.arange(N, dtype=edge_index.dtype)
        src = jnp.concatenate([edge_index[0], loops])
        dst = jnp.concatenate([edge_index[1], loops])
        h = h @ W_conv
        ones = jnp.ones(dst.shape[0], dtype=h.dtype)
        deg = jax.ops.segment_sum(ones, dst, num_segments=N)
        dinv = jnp.where(deg > 0, jax.lax.rsqrt(deg), 0.0)
        norm = dinv[src] * dinv[dst]
        msgs = norm[:, None] * h[src]
        out = jax.ops.segment_sum(msgs, dst, num_segments=N) + b_conv
        return jax.nn.relu(batchnorm(out, gamma2, beta2))

    def _L2_gnn_ref(x, edge_index, conv_w, att_src, att_dst, conv_b, proj_w, proj_b, skip_w, skip_b):
        import jax, jax.numpy as jnp
        import numpy as np
        N_NODES = 50000
        N_EDGES = 25000
        HIDDEN = 128
        HEADS = 4
        LAYERS = 2
        NEG_SLOPE = 0.2

        def _gat_layer(x, src, dst, W, a_s, a_d, b):
            N = x.shape[0]
            h = (x @ W).reshape(N, HEADS, HIDDEN)
            alpha_src = jnp.einsum('nhc,hc->nh', h, a_s)
            alpha_dst = jnp.einsum('nhc,hc->nh', h, a_d)
            alpha = alpha_src[src] + alpha_dst[dst]
            alpha = jnp.where(alpha >= 0, alpha, NEG_SLOPE * alpha)
            amax = jax.ops.segment_max(alpha, dst, num_segments=N)
            ex = jnp.exp(alpha - amax[dst])
            denom = jax.ops.segment_sum(ex, dst, num_segments=N)
            w = ex / (denom[dst] + 1e-16)
            msg = h[src] * w[:, :, None]
            out = jax.ops.segment_sum(msg, dst, num_segments=N)
            return out.mean(axis=1) + b
        src, dst = (edge_index[0], edge_index[1])
        out = x
        for l in range(LAYERS):
            conv = _gat_layer(out, src, dst, conv_w[l], att_src[l], att_dst[l], conv_b[l])
            out = jax.nn.relu(conv) @ proj_w[l] + proj_b[l] + (out @ skip_w[l] + skip_b[l])
        return out

    def _L3_gnn_ref(x, edge_index, edge_type, edge_weight, W1, root1, b1, W2, root2, b2):
        import jax, jax.numpy as jnp
        import numpy as np
        NUM_RELATIONS = 4
        N_NODES = 625
        N_EDGES = 10000
        F_IN = 128
        HID = 128
        EMB = 128

        def _rgcn_conv(x, src, dst, edge_type, edge_weight, W, root, bias):
            xj = x[src]
            m = jnp.zeros((xj.shape[0], W.shape[2]), dtype=x.dtype)
            for r in range(W.shape[0]):
                mask = (edge_type == r).astype(x.dtype)[:, None]
                m = m + mask * (xj @ W[r])
            m = m * edge_weight[:, None]
            out = jax.ops.segment_sum(m, dst, num_segments=x.shape[0])
            return out + x @ root + bias
        src, dst = (edge_index[0], edge_index[1])
        ew = (edge_weight - edge_weight.min()) / (edge_weight.max() - edge_weight.min() + 1e-08)
        h = jax.nn.relu(_rgcn_conv(x, src, dst, edge_type, ew, W1, root1, b1))
        h = _rgcn_conv(h, src, dst, edge_type, ew, W2, root2, b2)
        return h
    edge_index = jnp.stack([src, dst])
    x = _layernorm(x + _L0_gnn_ref(x, src, dst), axis=-1)
    x = _layernorm(x + _L1_gnn_ref(x, edge_index, L1_gnn_W_mlp, L1_gnn_b_mlp, L1_gnn_gamma1, L1_gnn_beta1, L1_gnn_W_conv, L1_gnn_b_conv, L1_gnn_gamma2, L1_gnn_beta2), axis=-1)
    x = _layernorm(x + _L2_gnn_ref(x, edge_index, L2_gnn_conv_w, L2_gnn_att_src, L2_gnn_att_dst, L2_gnn_conv_b, L2_gnn_proj_w, L2_gnn_proj_b, L2_gnn_skip_w, L2_gnn_skip_b), axis=-1)
    x = _layernorm(x + _L3_gnn_ref(x, edge_index, edge_type_4, edge_weight, L3_gnn_W1, L3_gnn_root1, L3_gnn_b1, L3_gnn_W2, L3_gnn_root2, L3_gnn_b2), axis=-1)
    return x

_drawn_inputs = setup_inputs


def setup_inputs(seed=0):
    import zlib

    import numpy as np

    out = dict(_drawn_inputs(seed))
    spreads = {'L1_gnn_gamma1': (1.0, 0.2),
     'L1_gnn_beta1': (0.0, 0.1),
     'L1_gnn_gamma2': (1.0, 0.2),
     'L1_gnn_beta2': (0.0, 0.1)}
    factors = {'L1_gnn_b_mlp': 8.0,
     'L1_gnn_b_conv': 8.0,
     'L2_gnn_att_dst': 3.061,
     'L2_gnn_conv_b': 5.436,
     'L2_gnn_proj_b': 3.369,
     'L2_gnn_skip_b': 2.872}
    for name, (base, spread) in spreads.items():
        noise = np.random.default_rng([zlib.crc32(name.encode()), seed]).standard_normal(out[name].shape)
        drawn = base * np.exp(spread * noise) if base else spread * noise
        out[name] = jnp.asarray(drawn.astype(out[name].dtype))
    for name, factor in factors.items():
        out[name] = (out[name] * factor).astype(out[name].dtype)
    return out
```

```python
from contextlib import ExitStack

import numpy as np
import concourse.bass as bass
import concourse.mybir as mybir

F32 = mybir.dt.float32
BF16 = mybir.dt.bfloat16
I32 = mybir.dt.int32
ALU = mybir.AluOpType
ACT = mybir.ActivationFunctionType
AX = mybir.AxisListType

P = 128
N, E, D = 3125, 50000, 128
NT = (N + P - 1) // P
NPAD = NT * P
LASTN = N - (NT - 1) * P
HEADS, REL, LAYERS = 4, 4, 2
ET = (E + P - 1) // P
ETP = 392
CH, RP = 4, 98
LASTE = E - (ET - 1) * P
W_WIDE, W_SLIM = 128, 32
WIN_WIDE = NPAD // W_WIDE
WIN_SLIM = (N + W_SLIM - 1) // W_SLIM
RING = 8
S_WIDE = 416
S_SLIM = 488
assert S_WIDE >= ET + WIN_WIDE - 1 and S_SLIM >= ET + WIN_SLIM - 1 and S_SLIM - ET < WIN_SLIM
FAR = 100000.0
BIG = 1.0e30
LN_EPS = BN_EPS = 1e-5
NEG_SLOPE = 0.2
UW = D + 1


class Signal:

    def __init__(self, nc, ctx, name):
        self.sem = ctx.enter_context(nc.semaphore(name))
        self.base = 0

    def at(self, count):
        return self.base + count

    def advance(self, count):
        self.base += count


class Chain:

    def __init__(self, signal):
        self.s = signal

    def mark(self, ins):
        ins.then_inc(self.s.sem, 1)
        self.s.base += 1
        return self.s.base

    def then_wait(self, eng, ins):
        eng.wait_ge(self.s.sem, self.mark(ins))


def bc(ap, axis, n):
    a = ap.unsqueeze(axis)
    shape = list(a.shape)
    shape[axis] = n
    return a.broadcast_to(tuple(shape))


class Net:
    pass


def load_all(nc, k, pairs, scattered=False):
    with nc.Block() as block:
        @block.sync
        def _(sp):
            for out, in_ in pairs:
                sp.dma_start(out, in_, allow_slow_non_contiguous=scattered).then_inc(k.moved.sem, 16)
            k.moved.advance(16 * len(pairs))
            sp.wait_ge(k.moved.sem, k.moved.base)


def banks(n):
    return [(a, min(512, n - a)) for a in range(0, n, 512)]


def turn(nc, k, pieces, evac):
    with nc.Block() as block:
        @block.tensor
        def _(pe):
            for col, src in pieces:
                rows, cols = src.shape
                last = pe.transpose(k.ps[0:cols, col:col + rows], src, k.ident[0:rows, 0:rows])
            last.then_inc(k.pe_done.sem, 1)
            k.pe_done.advance(1)

        @block.vector
        def _(dve):
            dve.wait_ge(k.pe_done.sem, k.pe_done.base)
            c = Chain(k.dve_step)
            for ins in evac(dve):
                c.then_wait(dve, ins)


def to_feature_major(nc, k, src, dst):
    def evac(dve):
        for a, m in banks(NPAD):
            yield dve.tensor_copy(dst[:, a:a + m], k.ps[:, a:a + m])
    turn(nc, k, [(i * P, src[:, i, :]) for i in range(NT)], evac)


def to_node_major(nc, k, src, dst):
    def evac(dve):
        flat = dst[:, :, :].rearrange("p i f -> p (i f)")
        for a, m in banks(NPAD):
            yield dve.tensor_copy(flat[:, a:a + m], k.ps[:, a:a + m])
    turn(nc, k, [(i * P, src[:, i * P:(i + 1) * P]) for i in range(NT)], evac)



def constants(nc, k):
    with nc.Block() as block:
        @block.gpsimd
        def _(pool):
            pool.iota(k.int_a[:, 0:P], pattern=[[1, P]], base=0, channel_multiplier=0)
            pool.iota(k.int_b[:, 0:1], pattern=[[0, 1]], base=0, channel_multiplier=1)
            pool.iota(k.int_b[:, 1:5], pattern=[[P, 4]], base=0, channel_multiplier=1)
            pool.iota(k.int_b[:, 5:5 + NT], pattern=[[P, NT]], base=0, channel_multiplier=1)
            pool.iota(k.int_c[:, 0:ETP], pattern=[[1, ETP]], base=0,
                      channel_multiplier=0).then_inc(k.pool_done.sem, 1)
            k.pool_done.advance(1)

        @block.vector
        def _(dve):
            c = Chain(k.dve_step)
            dve.memset(k.ones[:, :], 1.0)
            dve.memset(k.xN[:, NT - 1, :], 0.0)
            dve.memset(k.zeros[:, :], 0.0)
            dve.wait_ge(k.pool_done.sem, k.pool_done.base)
            c.then_wait(dve, dve.tensor_copy(k.iota_row[:, :], k.int_a[:, 0:P]))
            c.then_wait(dve, dve.tensor_copy(k.part_id[:, :], k.int_b[:, 0:1]))
            dve.tensor_copy(k.step_id[:, :], k.int_b[:, 1:5])
            dve.tensor_copy(k.node_id[:, :], k.int_b[:, 5:5 + NT])
            dve.tensor_copy(k.tile_id[:, :], k.int_c[0:1, 0:ETP])
            dve.tensor_copy(k.iota_bf[:, :], k.iota_row[:, :])
            dve.tensor_scalar(k.ident[:, :], k.iota_row[:, :], k.part_id[:, 0:1], None, ALU.is_equal)
            c.then_wait(dve, dve.tensor_scalar(k.before[:, :], k.iota_row[:, :], k.part_id[:, 0:1],
                                               None, ALU.is_gt))
    top = (NT - 1) * P
    load_all(nc, k, [
        (k.xN[:, 0:NT - 1, :], k.in_["x"][0:top, :].rearrange("(i p) f -> p i f", p=P)),
        (k.xN[0:LASTN, NT - 1, :], k.in_["x"][top:N, :])])


def edge_rows(nc, k, edF):
    with ExitStack() as ctx:
        raw = ctx.enter_context(nc.sbuf_tensor("edge_raw", [RP, 3, CH, P], I32))
        with nc.Block() as block:
            @block.vector
            def _(dve):
                c = Chain(k.dve_step)
                dve.memset(raw[:, 0:2, CH - 1, :], int(FAR))
                dve.memset(raw[:, 2, CH - 1, :], 0)
                c.then_wait(dve, dve.memset(edF[:, CH - 1, 3, :], 0.0))
        full = (CH - 1) * RP * P
        rest = (ET - 1) * P - full
        loads = []
        for a, name in enumerate(("dst", "src", "edge_type_4", "edge_weight")):
            flat = k.in_[name]
            out = raw[:, a, :, :] if a < 3 else edF[:, :, 3, :]
            loads += [
                (out[:, 0:CH - 1, :], flat[0:full].rearrange("(c p e) -> p c e", c=CH - 1, e=P)),
                (out[0:rest // P, CH - 1, :], flat[full:full + rest].rearrange("(p e) -> p e", e=P)),
                (out[rest // P:rest // P + 1, CH - 1, 0:LASTE],
                 flat[full + rest:E].rearrange("(p e) -> p e", p=1))]
        load_all(nc, k, loads)
        with nc.Block() as block:
            @block.vector
            def _(dve):
                c = Chain(k.dve_step)
                for a in range(3):
                    c.then_wait(dve, dve.tensor_copy(edF[:, :, a, :], raw[:, a, :, :]))
    load_all(nc, k, [(k.edges_d.rearrange("(c p) x -> p c x", c=CH),
                      edF[:, :, :, :].rearrange("p c a e -> p c (a e)"))])


def edge_columns(nc, k, edF, dstE, srcE):
    pieces = []
    for a in range(2):
        for c in range(CH):
            pieces.append((a * 512 + c * RP, edF[:, c, a, :]))

    def evac(dve):
        yield dve.tensor_copy(dstE[:, :], k.ps[:, 0:ETP])
        yield dve.tensor_copy(srcE[:, :], k.ps[:, 512:512 + ETP])
        yield dve.tensor_scalar(k.src_tile[:, :], srcE[:, :], float(N - 1), None, ALU.min)
    turn(nc, k, pieces, evac)


def degrees(nc, k, dstE, srcE):
    G = RING
    with ExitStack() as ctx:
        def sb(name, shape, dt):
            return ctx.enter_context(nc.sbuf_tensor(name, shape, dt))
        whole = sb("deg_int", [P, 2, ETP], I32)
        part = sb("deg_part", [P, 2, ETP], I32)
        lo = sb("deg_lo", [P, 2, ETP], BF16)
        hi = sb("deg_hi", [P, 2, ETP], BF16)
        hot_lo = sb("deg_hot_lo", [P, 2, G, P], BF16)
        hot_hi = sb("deg_hot_hi", [P, 2, G, NT], BF16)
        groups = ETP // G
        with nc.Block() as block:
            @block.vector
            def _(dve):
                c = Chain(k.dve_step)
                dve.tensor_copy(whole[:, 0, :], dstE[:, :])
                c.then_wait(dve, dve.tensor_copy(whole[:, 1, :], srcE[:, :]))
                c.then_wait(dve, dve.tensor_scalar(part[:, :, :], whole[:, :, :], P - 1, None,
                                                   ALU.bitwise_and))
                c.then_wait(dve, dve.tensor_copy(lo[:, :, :], part[:, :, :]))
                c.then_wait(dve, dve.tensor_scalar(part[:, :, :], whole[:, :, :], 7, None,
                                                   ALU.arith_shift_right))
                c.then_wait(dve, dve.tensor_copy(hi[:, :, :], part[:, :, :]))
                with dve.Fori(0, groups) as g:
                    for a in range(2):
                        dve.wait_ge(k.used[a].sem, k.used[a].at(1) + g)
                        dve.tensor_tensor(hot_lo[:, a, :, :], bc(lo[:, a, bass.ds(g * G, G)], 2, P),
                                          bc(k.iota_bf[:, :], 1, G), ALU.is_equal)
                        dve.tensor_tensor(hot_hi[:, a, :, :], bc(hi[:, a, bass.ds(g * G, G)], 2, NT),
                                          bc(k.iota_bf[:, 0:NT], 1, G),
                                          ALU.is_equal).then_inc(k.built[a].sem, 1)

            @block.tensor
            def _(pe):
                for a in range(2):
                    pe.sem_inc(k.used[a].sem, 1)
                for a in range(2):
                    pe.matmul(k.ps[:, a * 512:a * 512 + NT], k.zeros[:, :], k.zeros[:, 0:NT],
                              start=True, stop=False, skip_group_check=True)
                with pe.Fori(0, groups) as g:
                    for a in range(2):
                        pe.wait_ge(k.built[a].sem, k.built[a].at(1) + g)
                        for j in range(G):
                            ins = pe.matmul(k.ps[:, a * 512:a * 512 + NT], hot_lo[:, a, j, :],
                                            hot_hi[:, a, j, :], start=False, stop=False,
                                            skip_group_check=True)
                        ins.then_inc(k.used[a].sem, 1)
        for a in range(2):
            k.used[a].advance(groups + 1)
            k.built[a].advance(groups)
    with ExitStack() as ctx:
        deg = ctx.enter_context(nc.sbuf_tensor("deg", [P, 2, NT], F32))
        root = ctx.enter_context(nc.sbuf_tensor("deg_root", [P, 2, NT], F32))
        tot = ctx.enter_context(nc.sbuf_tensor("deg_tot", [P, 3, NT], F32))
        start = ctx.enter_context(nc.sbuf_tensor("deg_start", [P, 3, NT], F32))
        with nc.Block() as block:
            @block.vector
            def _(dve):
                c = Chain(k.dve_step)
                dve.tensor_copy(deg[:, 0, :], k.ps[:, 0:NT])
                c.then_wait(dve, dve.tensor_copy(deg[:, 1, :], k.ps[:, 512:512 + NT]))
        with nc.Block() as block:
            @block.tensor
            def _(pe):
                pe.matmul(k.ps[:, 1024:1024 + NT], k.before[:, :], deg[:, 0, :], start=True, stop=True)
                pe.matmul(k.ps[:, 1536:1536 + NT], k.ones[:, :], deg[:, 0, :], start=True,
                          stop=True).then_inc(k.pe_done.sem, 1)
                k.pe_done.advance(1)

            @block.scalar
            def _(act):
                act.activation(root[:, :, :], deg[:, :, :], ACT.Sqrt, bias=k.ones[:, 0:1],
                               scale=1.0).then_inc(k.act_done.sem, 1)
                k.act_done.advance(1)

            @block.vector
            def _(dve):
                c = Chain(k.dve_step)
                dve.wait_ge(k.act_done.sem, k.act_done.base)
                c.then_wait(dve, dve.reciprocal(k.norm[:, :, :], root[:, :, :]))
                dve.wait_ge(k.pe_done.sem, k.pe_done.base)
                c.then_wait(dve, dve.tensor_copy(tot[:, 0, :], k.ps[:, 1536:1536 + NT]))
                c.then_wait(dve, dve.memset(tot[:, 2, :], 1.0))
                c.then_wait(dve, dve.tensor_tensor_scan(tot[:, 1, :], tot[:, 2, :], tot[:, 0, :], 0.0,
                                                        ALU.mult, ALU.add))
                c.then_wait(dve, dve.tensor_tensor(start[:, 0, :], tot[:, 1, :], tot[:, 0, :],
                                                   ALU.subtract))
                c.then_wait(dve, dve.tensor_tensor(start[:, 0, :], start[:, 0, :],
                                                   k.ps[:, 1024:1024 + NT], ALU.add))
                c.then_wait(dve, dve.tensor_scalar(start[:, 1, :], k.node_id[:, :], float(ETP * P), None,
                                                   ALU.add))
                c.then_wait(dve, dve.tensor_tensor(start[:, 1, :], start[:, 1, :], start[:, 0, :],
                                                   ALU.subtract))
                c.then_wait(dve, dve.tensor_scalar(start[:, 2, :], deg[:, 0, :], 0.0, None,
                                                   ALU.is_equal))
                c.then_wait(dve, dve.tensor_tensor(start[:, 1, :], start[:, 1, :], start[:, 2, :],
                                                   ALU.mult))
                c.then_wait(dve, dve.tensor_tensor(start[:, 0, :], start[:, 0, :], start[:, 1, :],
                                                   ALU.add))
                c.then_wait(dve, dve.tensor_copy(k.first_edge[:, :], start[:, 0, :]))


def staircase(nc, k, window, shift, tile_of, win_row, col_width, tile_row):
    with ExitStack() as ctx:
        def sb(name, shape, dt):
            return ctx.enter_context(nc.sbuf_tensor(f"{name}{window}", shape, dt))
        last = sb("stair_last", [1, ETP], F32)
        key = sb("stair_key", [1, ETP], F32)
        key_i = sb("stair_key_i", [1, ETP], I32)
        below = sb("stair_below", [P, 4, ET], F32)
        tile_f = sb("stair_tile", [P, 4], F32)
        both = sb("stair_both", [P, 2, 4], I32)
        win_f = sb("stair_win", [P, 4], F32)
        load_all(nc, k, [(last[:, :], k.edges_d.rearrange("t x -> x t")[P - 1:P, :])],
                 scattered=True)
        with nc.Block() as block:
            @block.vector
            def _(dve):
                c = Chain(k.dve_step)
                c.then_wait(dve, dve.tensor_scalar(last[:, :], last[:, :], float(N - 1), None, ALU.min))
                c.then_wait(dve, dve.tensor_copy(key_i[:, :], last[:, :]))
                c.then_wait(dve, dve.tensor_scalar(key_i[:, :], key_i[:, :], shift, None,
                                                   ALU.arith_shift_right))
                c.then_wait(dve, dve.tensor_copy(key[:, :], key_i[:, :]))
                c.then_wait(dve, dve.tensor_tensor(key[:, :], key[:, :], k.tile_id[:, :], ALU.add))
        with nc.Block() as block:
            @block.tensor
            def _(pe):
                pe.matmul(k.ps[:, 0:ETP], k.ones[0:1, :], key[:, :], start=True,
                          stop=True).then_inc(k.pe_done.sem, 1)
                k.pe_done.advance(1)

            @block.vector
            def _(dve):
                c = Chain(k.dve_step)
                dve.wait_ge(k.pe_done.sem, k.pe_done.base)
                c.then_wait(dve, dve.tensor_tensor(below[:, :, :], bc(k.ps[:, 0:ET], 1, 4),
                                                   bc(k.step_id[:, :], 2, ET), ALU.is_lt))
                c.then_wait(dve, dve.tensor_reduce(tile_f[:, :], below[:, :, :], AX.X, ALU.add))
                c.then_wait(dve, dve.tensor_scalar(tile_f[:, :], tile_f[:, :], float(ET - 1), None,
                                                   ALU.min))
                c.then_wait(dve, dve.tensor_copy(tile_of[:, :], tile_f[:, :]))
                c.then_wait(dve, dve.tensor_tensor(win_f[:, :], k.step_id[:, :], tile_f[:, :],
                                                   ALU.subtract))
                c.then_wait(dve, dve.tensor_scalar(both[:, 0, :], win_f[:, :], float(col_width), None,
                                                   ALU.mult))
                c.then_wait(dve, dve.tensor_copy(both[:, 1, :], tile_f[:, :]))
        load_all(nc, k, [
            (k.stepi_d.rearrange("a (c p) -> p a c", p=P), both[:, :, :]),
            (k.stepf_d.rearrange("a (c p) -> p (a c)", p=P), win_f[:, :])], scattered=True)
        rows = [(win_row[:, :], k.stepi_d[0:1, :]), (k.win_f_row[:, :], k.stepf_d[0:1, :])]
        if tile_row is not None:
            rows.append((tile_row[:, :], k.stepi_d[1:2, :]))
        load_all(nc, k, rows)


def fetch_rows(nc, k, table, tile_of, dst):
    with nc.Block() as block:
        @block.gpsimd
        def _(pool):
            for c in range(4):
                pool.indirect_dma_start(dst[:, c, :], None, table,
                                        bass.IndirectOffsetOnAxis(ap=tile_of[:, c:c + 1], axis=0)
                                        ).then_inc(k.fetched.sem, 16)
            k.fetched.advance(64)
            pool.wait_ge(k.fetched.sem, k.fetched.base)


def step_edges(nc, k, window, tile_of, local, wide):
    with ExitStack() as ctx:
        rows = ctx.enter_context(nc.sbuf_tensor(f"step_rows{window}", [P, 4, 512], F32))
        base = ctx.enter_context(nc.sbuf_tensor(f"step_base{window}", [P, 512], F32))
        tmp = ctx.enter_context(nc.sbuf_tensor(f"step_tmp{window}", [P, 512], F32))
        fetch_rows(nc, k, k.edges_d, tile_of, rows)
        with nc.Block() as block:
            @block.tensor
            def _(pe):
                pe.matmul(k.ps[:, 2048:2560], k.ones[0:1, :], k.win_f_row[:, :], start=True, stop=True)
                for a in range(4 if wide else 1):
                    for c in range(4):
                        ins = pe.transpose(k.ps[:, a * 512 + c * P:a * 512 + (c + 1) * P],
                                           rows[:, c, a * P:(a + 1) * P], k.ident[:, :])
                ins.then_inc(k.pe_done.sem, 1)
                k.pe_done.advance(1)

            @block.vector
            def _(dve):
                c = Chain(k.dve_step)
                dve.wait_ge(k.pe_done.sem, k.pe_done.base)
                c.then_wait(dve, dve.tensor_scalar(base[:, :], k.ps[:, 2048:2560], float(window), None,
                                                   ALU.mult))
                c.then_wait(dve, dve.tensor_tensor(local[:, :], k.ps[:, 0:512], base[:, :],
                                                   ALU.subtract))
                if wide:
                    c.then_wait(dve, dve.tensor_scalar(tmp[:, :], k.ps[:, 512:1024], float(N - 1), None,
                                                       ALU.min))
                    c.then_wait(dve, dve.tensor_copy(k.src_step[:, :], tmp[:, :]))
                    c.then_wait(dve, dve.tensor_scalar(tmp[:, :], tmp[:, :], float(REL), None, ALU.mult))
                    c.then_wait(dve, dve.tensor_tensor(k.rel_step[:, :], tmp[:, :], k.ps[:, 1024:1536],
                                                       ALU.add))
                    c.then_wait(dve, dve.tensor_copy(k.weight_step[:, :], k.ps[:, 1536:2048]))



def aggregate(nc, k, table, index, weight, init):
    groups = S_WIDE // RING
    H = RING // 2
    with ExitStack() as ctx:
        def sb(name, shape, dt):
            return ctx.enter_context(nc.sbuf_tensor(f"{name}_{k.tag()}", shape, dt))
        rows = sb("agg_rows", [P, RING, D], F32)
        hot = sb("agg_hot", [P, RING, P], F32)
        idx = sb("agg_idx", [P, RING], I32)
        with nc.Block() as block:
            @block.gpsimd
            def _(pool):
                with pool.Fori(0, groups) as g:
                    for j in range(RING):
                        if j % H == 0:
                            pool.wait_ge(k.idx_ready.sem, k.idx_ready.at(j // H + 1) + g * 2)
                            pool.sem_inc(k.tick.sem, 1)
                        pool.indirect_dma_start(rows[:, j, :], None, table,
                                                bass.IndirectOffsetOnAxis(ap=idx[:, j:j + 1], axis=0)
                                                ).then_inc(k.row_in[j].sem, 16)

            @block.vector
            def _(dve):
                with dve.Fori(0, groups) as g:
                    for h in range(2):
                        cols = bass.ds(g * RING + h * H, H)
                        out = hot[:, h * H:(h + 1) * H, :]
                        dve.wait_ge(k.used[0].sem, k.used[0].at((h + 1) * H) + g * RING)
                        dve.tensor_copy(idx[:, h * H:(h + 1) * H], index[:, cols]).then_inc(
                            k.idx_ready.sem, 1)
                        ins = dve.tensor_tensor(out, bc(k.local_wide[:, cols], 2, P),
                                                bc(k.iota_row[:, :], 1, H), ALU.is_equal)
                        if weight is not None:
                            ins.then_inc(k.part.sem, 1)
                            dve.wait_ge(k.part.sem, k.part.at(h + 1) + g * 2)
                            ins = dve.tensor_tensor(out, out, bc(weight[:, cols], 2, P), ALU.mult)
                        ins.then_inc(k.built[h].sem, 1)

            @block.tensor
            def _(pe):
                pe.sem_inc(k.used[0].sem, RING)
                init(pe)
                with pe.Fori(0, groups) as g:
                    for j in range(RING):
                        col = pe.value_load(k.win_wide[0:1, bass.ds(g * RING + j, 1)], min_val=0,
                                            max_val=WIN_WIDE * P)
                        if j % H == 0:
                            pe.wait_ge(k.built[j // H].sem, k.built[j // H].at(1) + g)
                        pe.wait_ge(k.row_in[j].sem, k.row_in[j].at(16) + g * 16)
                        pe.matmul(k.ps[:, bass.ds(col, D)], hot[:, j, :], rows[:, j, :], start=False,
                                  stop=False, skip_group_check=True).then_inc(k.used[0].sem, 1)
        k.idx_ready.advance(2 * groups)
        k.tick.advance(2 * groups)
        k.used[0].advance(RING + S_WIDE)
        for j in range(RING):
            k.row_in[j].advance(16 * groups)
        for h in range(2):
            k.built[h].advance(groups)
        if weight is not None:
            k.part.advance(2 * groups)


def init_self(k, own):
    def init(pe):
        for i in range(NT + 1):
            rhs = own[:, i, :] if i < NT else k.zeros[:, :]
            pe.matmul(k.ps[:, i * P:(i + 1) * P], k.ident[:, :], rhs, start=(i % 4 == 0), stop=False,
                      skip_group_check=True)
    return init


def init_root(k, xT, root, bias):
    def init(pe):
        for i in range(NT + 1):
            lhs = xT[:, i * P:(i + 1) * P] if i < NT else k.zeros[:, :]
            pe.matmul(k.ps[:, i * P:(i + 1) * P], lhs, root, start=(i % 4 == 0), stop=False,
                      skip_group_check=True)
            pe.matmul(k.ps[:, i * P:(i + 1) * P], k.ones[0:1, :], bias, start=False, stop=False,
                      skip_group_check=True)
    return init


def layernorm(nc, k, y, out):
    with ExitStack() as ctx:
        tag = k.tag()
        sq = ctx.enter_context(nc.sbuf_tensor(f"ln_sq_{tag}", [P, NT, D], F32))
        st = ctx.enter_context(nc.sbuf_tensor(f"ln_st_{tag}", [P, 4, NT], F32))
        with nc.Block() as block:
            @block.vector
            def _(dve):
                c = Chain(k.dve_step)
                c.then_wait(dve, dve.tensor_reduce(st[:, 0, :], y[:, :, :], AX.X, ALU.add))
                c.then_wait(dve, dve.tensor_scalar(st[:, 0, :], st[:, 0, :], 1.0 / D, None, ALU.mult))
                c.then_wait(dve, dve.tensor_tensor(y[:, :, :], y[:, :, :], bc(st[:, 0, :], 2, D),
                                                   ALU.subtract))
                c.then_wait(dve, dve.tensor_tensor(sq[:, :, :], y[:, :, :], y[:, :, :], ALU.mult))
                c.then_wait(dve, dve.tensor_reduce(st[:, 1, :], sq[:, :, :], AX.X, ALU.add))
                dve.tensor_scalar(st[:, 2, :], st[:, 1, :], 1.0 / D, LN_EPS, ALU.mult,
                                  ALU.add).then_inc(k.dve_done.sem, 1)
                k.dve_done.advance(1)
                dve.wait_ge(k.act_done.sem, k.act_done.at(1))
                c.then_wait(dve, dve.reciprocal(st[:, 0, :], st[:, 3, :]))
                c.then_wait(dve, dve.tensor_tensor(out[:, :, :], y[:, :, :], bc(st[:, 0, :], 2, D),
                                                   ALU.mult))

            @block.scalar
            def _(act):
                act.wait_ge(k.dve_done.sem, k.dve_done.base)
                act.activation(st[:, 3, :], st[:, 2, :], ACT.Sqrt).then_inc(k.act_done.sem, 1)
                k.act_done.advance(1)


def vector_ops(nc, k, ops):
    with nc.Block() as block:
        @block.vector
        def _(dve):
            c = Chain(k.dve_step)
            for ins in ops(dve):
                c.then_wait(dve, ins)


def acc_view(k):
    return k.ps[:, 0:NPAD].rearrange("p (i f) -> p i f", f=D)



def layer0(nc, k):
    with ExitStack() as ctx:
        xs = ctx.enter_context(nc.sbuf_tensor("l0_xs", [P, NT, D], F32))
        vector_ops(nc, k, lambda dve: iter([dve.tensor_tensor(
            xs[:, :, :], k.xN[:, :, :], bc(k.norm[:, 0, :], 2, D), ALU.mult)]))
        load_all(nc, k, [(k.rows_d.rearrange("(i p) f -> p i f", p=P), xs[:, :, :])])
        aggregate(nc, k, k.rows_d, k.src_step, None, init_self(k, xs))

        def ops(dve):
            yield dve.tensor_tensor(xs[:, :, :], acc_view(k), bc(k.norm[:, 1, :], 2, D), ALU.mult)
            yield dve.tensor_tensor(xs[:, :, :], xs[:, :, :], k.xN[:, :, :], ALU.add)
        vector_ops(nc, k, ops)
        layernorm(nc, k, xs, k.xN)
    to_feature_major(nc, k, k.xN, k.xT)



def batchnorm_relu(nc, k, src, gamma, beta, out, st):
    parts = banks(N)
    with nc.Block() as block:
        @block.vector
        def _(dve):
            c = Chain(k.dve_step)
            for j, (a, m) in enumerate(parts):
                c.then_wait(dve, dve.bn_stats(st[:, 6 * j:6 * j + 6], src[:, a:a + m]))
            mv, sd, sc, sh = st[:, 48:50], st[:, 50:51], st[:, 51:52], st[:, 52:53]
            c.then_wait(dve, dve.bn_aggr(mv, st[:, 0:6 * len(parts)]))
            dve.tensor_scalar(sd, mv[:, 1:2], BN_EPS, None, ALU.add).then_inc(k.dve_done.sem, 1)
            k.dve_done.advance(1)
            dve.wait_ge(k.act_done.sem, k.act_done.at(1))
            c.then_wait(dve, dve.reciprocal(st[:, 54:55], st[:, 53:54]))
            c.then_wait(dve, dve.tensor_tensor(sc, st[:, 54:55], gamma, ALU.mult))
            c.then_wait(dve, dve.tensor_tensor(sh, mv[:, 0:1], sc, ALU.mult))
            dve.tensor_tensor(sh, beta, sh, ALU.subtract).then_inc(k.dve_done.sem, 1)
            k.dve_done.advance(1)

        @block.scalar
        def _(act):
            act.wait_ge(k.dve_done.sem, k.dve_done.base - 1)
            act.activation(st[:, 53:54], st[:, 50:51], ACT.Sqrt).then_inc(k.act_done.sem, 1)
            act.wait_ge(k.dve_done.sem, k.dve_done.base)
            act.activation(out[:, 0:NPAD], src[:, 0:NPAD], ACT.Relu, bias=st[:, 52:53],
                           scale=st[:, 51:52]).then_inc(k.act_done.sem, 1)
            k.act_done.advance(2)
            act.wait_ge(k.act_done.sem, k.act_done.base)


def layer1(nc, k):
    with ExitStack() as ctx:
        def sb(name, shape):
            return ctx.enter_context(nc.sbuf_tensor("l1_" + name, shape, F32))
        w_mlp, w_conv = sb("w_mlp", [P, D]), sb("w_conv", [P, D])
        cols = sb("cols", [P, 6])
        hT = sb("hT", [P, NPAD])
        hN = sb("hN", [P, NT, D])
        st = sb("st", [P, 64])
        names = ["b_mlp", "gamma1", "beta1", "b_conv", "gamma2", "beta2"]
        load_all(nc, k, [(w_mlp[:, :], k.in_["L1_gnn_W_mlp"]), (w_conv[:, :], k.in_["L1_gnn_W_conv"])]
                 + [(cols[:, j:j + 1], k.in_["L1_gnn_" + n].rearrange("(p a) -> p a", a=1))
                    for j, n in enumerate(names)])
        with nc.Block() as block:
            @block.tensor
            def _(pe):
                for a, m in banks(NPAD):
                    pe.matmul(k.ps[:, a:a + m], w_mlp[:, :], k.xT[:, a:a + m], start=True,
                              stop=True).then_inc(k.pe_done.sem, 1)

            @block.scalar
            def _(act):
                for j, (a, m) in enumerate(banks(NPAD)):
                    act.wait_ge(k.pe_done.sem, k.pe_done.at(j + 1))
                    act.activation(hT[:, a:a + m], k.ps[:, a:a + m], ACT.Identity,
                                   bias=cols[:, 0:1]).then_inc(k.act_done.sem, 1)
                k.pe_done.advance(len(banks(NPAD)))
                k.act_done.advance(len(banks(NPAD)))
                act.wait_ge(k.act_done.sem, k.act_done.base)
        batchnorm_relu(nc, k, hT, cols[:, 1:2], cols[:, 2:3], hT, st)
        with nc.Block() as block:
            @block.tensor
            def _(pe):
                for i in range(NT):
                    ins = pe.matmul(k.ps[:, i * P:(i + 1) * P], hT[:, i * P:(i + 1) * P], w_conv[:, :],
                                    start=True, stop=True)
                ins.then_inc(k.pe_done.sem, 1)
                k.pe_done.advance(1)

            @block.vector
            def _(dve):
                dve.wait_ge(k.pe_done.sem, k.pe_done.base)
                c = Chain(k.dve_step)
                c.then_wait(dve, dve.tensor_tensor(hN[:, :, :], acc_view(k), bc(k.norm[:, 0, :], 2, D),
                                                   ALU.mult))
        load_all(nc, k, [(k.rows_d.rearrange("(i p) f -> p i f", p=P), hN[:, :, :])])
        aggregate(nc, k, k.rows_d, k.src_step, None, init_self(k, hN))
        vector_ops(nc, k, lambda dve: iter([dve.tensor_tensor(
            hN[:, :, :], acc_view(k), bc(k.norm[:, 0, :], 2, D), ALU.mult)]))

        def evac(dve):
            for a, m in banks(NPAD):
                yield dve.tensor_scalar(hT[:, a:a + m], k.ps[:, a:a + m], cols[:, 3:4], None, ALU.add)
        turn(nc, k, [(i * P, hN[:, i, :]) for i in range(NT)], evac)
        batchnorm_relu(nc, k, hT, cols[:, 4:5], cols[:, 5:6], hT, st)
        to_node_major(nc, k, hT, hN)
        vector_ops(nc, k, lambda dve: iter([dve.tensor_tensor(
            hN[:, :, :], hN[:, :, :], k.xN[:, :, :], ALU.add)]))
        layernorm(nc, k, hN, k.xN)
    to_feature_major(nc, k, k.xN, k.xT)



def flags(nc, k, edF, keep, res_f, res_b):
    with ExitStack() as ctx:
        one = ctx.enter_context(nc.sbuf_tensor("flag_one", [RP, CH, P], F32))
        two = ctx.enter_context(nc.sbuf_tensor("flag_two", [RP, CH, P], F32))
        ends = ctx.enter_context(nc.sbuf_tensor("flag_ends", [HEADS, 2, ETP], F32))
        ft = ctx.enter_context(nc.sbuf_tensor("flag_tmp", [HEADS, 2, ETP], F32))
        by_x = k.edges_d.rearrange("t x -> x t")
        load_all(nc, k, [(ends[h:h + 1, a, :], by_x[col:col + 1, :])
                         for h in range(HEADS) for a, col in enumerate((0, P - 1))],
                 scattered=True)

        def ops(dve):
            dst = edF[:, :, 0, :]
            yield dve.memset(one[:, :, 0:1], 0.0)
            yield dve.memset(two[:, :, P - 1:P], 0.0)
            yield dve.tensor_tensor(one[:, :, 1:P], dst[:, :, 1:P], dst[:, :, 0:P - 1], ALU.is_equal)
            yield dve.tensor_tensor(two[:, :, 0:P - 1], dst[:, :, 1:P], dst[:, :, 0:P - 1],
                                    ALU.is_equal)
            yield dve.tensor_copy(keep[:, :, :, :], bc(one[:, :, :], 2, HEADS))
            yield dve.tensor_scalar(one[:, :, :], one[:, :, :], 1.0, BIG, ALU.subtract, ALU.mult)
            yield dve.tensor_scalar(two[:, :, :], two[:, :, :], 1.0, BIG, ALU.subtract, ALU.mult)
            yield dve.tensor_copy(res_f[:, :, :, :], bc(one[:, :, :], 2, HEADS))
            yield dve.tensor_copy(res_b[:, :, :, :], bc(two[:, :, :], 2, HEADS))
            single, joined = ft[:, 0, :], ft[:, 1, :]
            yield dve.memset(k.chain[:, :, :], 0.0)
            yield dve.memset(joined[:, 0:1], 0.0)
            yield dve.tensor_tensor(single, ends[:, 0, :], ends[:, 1, :], ALU.is_equal)
            yield dve.tensor_tensor(joined[:, 1:ETP], ends[:, 0, 1:ETP], ends[:, 1, 0:ETP - 1],
                                    ALU.is_equal)
            yield dve.tensor_tensor(k.chain[:, 0, :], single, joined, ALU.mult)
            yield dve.tensor_copy(k.chain[:, 1, :], joined)
            yield dve.tensor_tensor(k.chain[:, 2, 0:ETP - 1], single[:, 0:ETP - 1], joined[:, 1:ETP],
                                    ALU.mult)
            yield dve.tensor_scalar(k.chain[:, :, :], k.chain[:, :, :], 1.0, BIG, ALU.subtract, ALU.mult)
        vector_ops(nc, k, ops)


def fetch_attention(nc, k, asE):
    groups = ETP // RING
    H = RING // 2
    with ExitStack() as ctx:
        tag = k.tag()
        rows = ctx.enter_context(nc.sbuf_tensor(f"gat_rows_{tag}", [P, RING, D + HEADS], F32))
        idx = ctx.enter_context(nc.sbuf_tensor(f"gat_idx_{tag}", [P, RING], I32))
        spill = k.spill_d.rearrange("(t e) f -> e t f", e=P)
        with nc.Block() as block:
            @block.gpsimd
            def _(pool):
                with pool.Fori(0, groups) as g:
                    for h in range(2):
                        pool.wait_ge(k.idx_ready.sem, k.idx_ready.at(h + 1) + g * 2)
                        pool.sem_inc(k.tick.sem, 1)
                        pool.wait_ge(k.spilled[h].sem, k.spilled[h].at(16) + g * 16)
                        pool.sem_inc(k.tick.sem, 1)
                        pool.wait_ge(k.used[h].sem, k.used[h].at(1) + g)
                        pool.sem_inc(k.tick.sem, 1)
                        for j in range(h * H, (h + 1) * H):
                            pool.indirect_dma_start(
                                rows[:, j, :], None, k.scored_d,
                                bass.IndirectOffsetOnAxis(ap=idx[:, j:j + 1], axis=0)
                            ).then_inc(k.row_in[j].sem, 16)

            @block.vector
            def _(dve):
                with dve.Fori(0, groups) as g:
                    for h in range(2):
                        for j in range(h * H, (h + 1) * H):
                            dve.wait_ge(k.row_in[j].sem, k.row_in[j].at(0) + g * 16)
                        dve.tensor_copy(idx[:, h * H:(h + 1) * H],
                                        k.src_tile[:, bass.ds(g * RING + h * H, H)]).then_inc(
                            k.idx_ready.sem, 1)

            @block.sync
            def _(sp):
                for h in range(2):
                    sp.sem_inc(k.spilled[h].sem, 16)
                with sp.Fori(0, groups) as g:
                    for h in range(2):
                        for j in range(h * H, (h + 1) * H):
                            sp.wait_ge(k.row_in[j].sem, k.row_in[j].at(16) + g * 16)
                        sp.dma_start(spill[:, bass.ds(g * RING + h * H, H), :],
                                     rows[:, h * H:(h + 1) * H, 0:D]).then_inc(k.spilled[h].sem, 16)
                for h in range(2):
                    sp.wait_ge(k.spilled[h].sem, k.spilled[h].at(16 + 16 * groups))

            @block.scalar
            def _(act):
                for h in range(2):
                    act.sem_inc(k.used[h].sem, 1)
                with act.Fori(0, groups) as g:
                    for h in range(2):
                        for j in range(h * H, (h + 1) * H):
                            act.wait_ge(k.row_in[j].sem, k.row_in[j].at(16) + g * 16)
                        act.copy(asE[:, bass.ds(g * RING + h * H, H), :],
                                 rows[:, h * H:(h + 1) * H, D:D + HEADS]).then_inc(k.used[h].sem, 1)
                for h in range(2):
                    act.wait_ge(k.used[h].sem, k.used[h].at(1 + groups))
        k.idx_ready.advance(2 * groups)
        k.tick.advance(groups * 6)
        for h in range(2):
            k.spilled[h].advance(16 + 16 * groups)
            k.used[h].advance(1 + groups)
        for j in range(RING):
            k.row_in[j].advance(16 * groups)


def edge_weights(nc, k, asE, exS, keep, res_f, res_b):
    FREE = CH * HEADS * P
    with ExitStack() as ctx:
        tag = k.tag()

        def sb(name, shape, dt=F32):
            return ctx.enter_context(nc.sbuf_tensor(f"ew_{name}_{tag}", shape, dt))

        def flat(t):
            return t[:, :, :, :].rearrange("p c h e -> p (c h e)")

        def back(t):
            return flat(t)[:, ::-1]
        u = sb("u", [RP, CH, HEADS, P])
        v = sb("v", [RP, CH, HEADS, P])
        fwd = sb("fwd", [RP, CH, HEADS, P])
        bwd = sb("bwd", [RP, CH, HEADS, P])
        firsts = sb("firsts", [RP, CH, HEADS])
        starts = sb("starts", [RP, CH, P, HEADS])
        ends = sb("ends", [HEADS, 2, ETP])
        run = sb("run", [HEADS, 2, ETP])
        carry = sb("carry", [HEADS, 2, ETP])
        load_all(nc, k, [(starts[:, :, :, :].rearrange("p c e h -> p c (e h)"),
                          k.start_d[0:ETP * P, :].rearrange("(c p e) h -> p c (e h)", c=CH, e=P))])
        with nc.Block() as block:
            @block.gpsimd
            def _(pool):
                for c in range(CH):
                    pool.indirect_dma_start(firsts[:, c, :], None, k.target_d,
                                            bass.IndirectOffsetOnAxis(ap=k.first_dst[:, c:c + 1],
                                                                      axis=0)
                                            ).then_inc(k.fetched.sem, 16)
                k.fetched.advance(16 * CH)
                pool.wait_ge(k.fetched.sem, k.fetched.base)

        def evac(dve):
            yield dve.tensor_copy(flat(u), k.ps[0:RP, 0:FREE])
            yield dve.tensor_copy(v[:, :, :, :], starts[:, :, :, :].rearrange("p c e h -> p c h e"))
            yield dve.tensor_copy(v[:, :, :, 0:1].rearrange("p c h e -> p c (h e)"), firsts[:, :, :])
            yield dve.tensor_tensor_scan(flat(fwd), flat(res_f), flat(u), -BIG, ALU.add, ALU.max)
            yield dve.tensor_tensor_scan(back(bwd), back(res_b), back(u), -BIG, ALU.add, ALU.max)
        turn(nc, k, [((c * HEADS + h) * P, asE[:, c * RP:(c + 1) * RP, h])
                     for c in range(CH) for h in range(HEADS)], evac)

        def chain(dve):
            yield dve.tensor_copy(ends[:, 0, :], k.ps[0:HEADS, 0:ETP])
            yield dve.tensor_copy(ends[:, 1, :], k.ps[0:HEADS, 512:512 + ETP])
            yield dve.tensor_tensor_scan(run[:, 0, :], k.chain[:, 0, :], ends[:, 0, :], -BIG, ALU.add,
                                         ALU.max)
            yield dve.tensor_tensor_scan(run[:, 1, ::-1], k.chain[:, 2, ::-1], ends[:, 1, ::-1], -BIG,
                                         ALU.add, ALU.max)
            yield dve.memset(carry[:, :, :], -BIG)
            yield dve.tensor_tensor(carry[:, 0, 1:ETP], run[:, 0, 0:ETP - 1], k.chain[:, 1, 1:ETP],
                                    ALU.add)
            yield dve.tensor_tensor(carry[:, 1, 0:ETP - 1], run[:, 1, 1:ETP], k.chain[:, 1, 1:ETP],
                                    ALU.add)
        turn(nc, k, [(c * RP, fwd[:, c, :, P - 1]) for c in range(CH)]
             + [(512 + c * RP, bwd[:, c, :, 0]) for c in range(CH)], chain)

        def finish(dve):
            for c in range(CH):
                for a, e in ((0, 0), (1, P - 1)):
                    col = (a * CH + c) * HEADS
                    yield dve.tensor_tensor(u[:, c, :, e], u[:, c, :, e], k.ps[0:RP, col:col + HEADS],
                                            ALU.max)
            yield dve.tensor_tensor_scan(flat(fwd), flat(res_f), flat(u), -BIG, ALU.add, ALU.max)
            yield dve.tensor_tensor_scan(back(bwd), back(res_b), back(u), -BIG, ALU.add, ALU.max)
            yield dve.tensor_tensor(flat(bwd), flat(fwd), flat(bwd), ALU.max)
            yield dve.tensor_tensor_scan(flat(fwd), flat(keep), flat(v), 0.0, ALU.mult, ALU.add)
            yield dve.tensor_tensor(flat(bwd), flat(bwd), flat(fwd), ALU.add)
            yield dve.scalar_tensor_tensor(flat(bwd), flat(bwd), NEG_SLOPE, flat(bwd), ALU.mult,
                                           ALU.max)
        turn(nc, k, [((a * CH + c) * HEADS, carry[:, a, c * RP:(c + 1) * RP])
                     for a in range(2) for c in range(CH)], finish)

        def scores(dve):
            yield dve.tensor_tensor(flat(u), k.ps[0:RP, 0:FREE], flat(fwd), ALU.add)
            yield dve.scalar_tensor_tensor(flat(u), flat(u), NEG_SLOPE, flat(u), ALU.mult, ALU.max)
            yield dve.tensor_tensor(flat(u), flat(u), flat(bwd), ALU.subtract)
        turn(nc, k, [((c * HEADS + h) * P, asE[:, c * RP:(c + 1) * RP, h])
                     for c in range(CH) for h in range(HEADS)], scores)
        with nc.Block() as block:
            @block.scalar
            def _(act):
                act.activation(flat(v), flat(u), ACT.Exp).then_inc(k.act_done.sem, 1)
                k.act_done.advance(1)
                act.wait_ge(k.act_done.sem, k.act_done.base)
        load_all(nc, k, [(k.exp_d.rearrange("(c p) x -> p c x", c=CH),
                          v[:, :, :, :].rearrange("p c h e -> p c (h e)"))])
    with ExitStack() as ctx:
        rows = ctx.enter_context(nc.sbuf_tensor(f"ew_rows_{k.tag()}", [P, 4, 512], F32))
        fetch_rows(nc, k, k.exp_d, k.tile_slim, rows)

        def evac2(dve):
            for h in range(HEADS):
                yield dve.tensor_copy(exS[:, h, :], k.ps[:, h * 512:(h + 1) * 512])
        turn(nc, k, [(h * 512 + c * P, rows[:, c, h * P:(h + 1) * P])
                     for h in range(HEADS) for c in range(4)], evac2)


def attend(nc, k, exS, U):
    groups = S_SLIM // RING
    H = RING // 2
    with ExitStack() as ctx:
        tag = k.tag()

        def sb(name, shape, dt=F32):
            return ctx.enter_context(nc.sbuf_tensor(f"at_{name}_{tag}", shape, dt))
        rows = sb("rows", [P, RING, D + HEADS])
        hot = sb("hot", [P, RING, W_SLIM])
        mat = sb("mat", [P, RING, HEADS, W_SLIM])
        Uf = U[:, :, :].rearrange("p w f -> p (w f)")
        with nc.Block() as block:
            @block.vector
            def _(dve):
                c = Chain(k.dve_step)
                dve.memset(Uf, 0.0)
                c.then_wait(dve, dve.memset(rows[:, :, D:D + 1], 1.0))
        with nc.Block() as block:
            def loader(first):
                def run(eng):
                    with eng.Fori(0, groups) as g:
                        for j in range(first, RING, 2):
                            t = eng.value_load(k.tile_slim_row[0:1, bass.ds(g * RING + j, 1)],
                                               min_val=0, max_val=ET - 1)
                            eng.wait_ge(k.used[0].sem, k.used[0].at(j + 1) + g * RING)
                            eng.dma_start(rows[:, j, 0:D], k.spill_d[bass.ds(t * P, P), :]).then_inc(
                                k.row_load[j].sem, 16)
                return run
            block.sync(loader(0))
            block.scalar(loader(1))

            @block.gpsimd
            def _(pool):
                with pool.Fori(0, groups) as g:
                    for h in range(2):
                        pool.wait_ge(k.used[0].sem, k.used[0].at((h + 1) * H) + g * RING)
                        pool.sem_inc(k.tick.sem, 1)
                        pool.wait_ge(k.part.sem, k.part.at(h + 1) + g * 2)
                        ex = exS[:, :, bass.ds(g * RING + h * H, H)].rearrange("p h s -> p s h")
                        pool.tensor_tensor(mat[:, h * H:(h + 1) * H, :, :],
                                           bc(hot[:, h * H:(h + 1) * H, :], 2, HEADS),
                                           bc(ex, 3, W_SLIM), ALU.mult).then_inc(k.built[h].sem, 1)

            @block.tensor
            def _(pe):
                pe.sem_inc(k.used[0].sem, RING)
                pe.sem_inc(k.added.sem, RING)
                with pe.Fori(0, groups) as g:
                    for j in range(RING):
                        if j % H == 0:
                            pe.wait_ge(k.built[j // H].sem, k.built[j // H].at(1) + g)
                        pe.wait_ge(k.row_load[j].sem, k.row_load[j].at(16) + g * 16)
                        pe.wait_ge(k.added.sem, k.added.at(j + 1) + g * RING)
                        pe.matmul(k.ps[:, j * 512:j * 512 + UW],
                                  mat[:, j, :, :].rearrange("p h w -> p (h w)"), rows[:, j, 0:UW],
                                  start=True, stop=True).then_inc(k.used[0].sem, 1)

            @block.vector
            def _(dve):
                with dve.Fori(0, groups) as g:
                    for h in range(2):
                        dve.wait_ge(k.used[0].sem, k.used[0].at((h + 1) * H) + g * RING)
                        dve.tensor_tensor(hot[:, h * H:(h + 1) * H, :],
                                          bc(k.local_slim[:, bass.ds(g * RING + h * H, H)], 2, W_SLIM),
                                          bc(k.iota_row[:, 0:W_SLIM], 1, H),
                                          ALU.is_equal).then_inc(k.part.sem, 1)
                    for j in range(RING):
                        col = dve.value_load(k.win_slim[0:1, bass.ds(g * RING + j, 1)], min_val=0,
                                             max_val=(WIN_SLIM - 1) * UW)
                        dve.wait_ge(k.used[0].sem, k.used[0].at(RING + j + 1) + g * RING)
                        dve.wait_ge(k.added.sem, k.added.at(RING + j) + g * RING)
                        dve.tensor_tensor(Uf[:, bass.ds(col, UW)], k.ps[:, j * 512:j * 512 + UW],
                                          Uf[:, bass.ds(col, UW)], ALU.add).then_inc(k.added.sem, 1)
                dve.wait_ge(k.added.sem, k.added.at(RING + S_SLIM))
        k.used[0].advance(RING + S_SLIM)
        k.added.advance(RING + S_SLIM)
        k.part.advance(2 * groups)
        k.tick.advance(2 * groups)
        for h in range(2):
            k.built[h].advance(groups)
        for j in range(RING):
            k.row_load[j].advance(16 * groups)


def layer2(nc, k, edF):
    with ExitStack() as outer:
        def so(name, shape, dt=F32):
            return outer.enter_context(nc.sbuf_tensor("l2_" + name, shape, dt))
        keep = so("keep", [RP, CH, HEADS, P])
        res_f = so("res_f", [RP, CH, HEADS, P])
        res_b = so("res_b", [RP, CH, HEADS, P])
        gN = so("gN", [P, NT, D])
        exS = so("exS", [P, HEADS, 512])
        conv_w = so("conv_w", [P, HEADS * D])
        proj_w, skip_w = so("proj_w", [P, D]), so("skip_w", [P, D])
        col = so("col", [P, 4])
        score_w = so("score_w", [P, 2 * HEADS])
        flags(nc, k, edF, keep, res_f, res_b)
        with ExitStack() as ctx:
            zero = ctx.enter_context(nc.sbuf_tensor("l2_zero", [P, ETP * HEADS], F32))
            vector_ops(nc, k, lambda dve: iter([dve.memset(zero[:, :], 0.0)]))
            load_all(nc, k, [(k.start_d[0:ETP * P, :].rearrange("(p t) h -> p (t h)", p=P),
                              zero[:, :])])
        gT = k.xT
        for layer in range(LAYERS):
            own = k.xN if layer == 0 else gN
            with ExitStack() as ctx:
                tag = k.tag()

                def sb(name, shape, dt=F32):
                    return ctx.enter_context(nc.sbuf_tensor(f"l2_{name}_{tag}", shape, dt))
                att = sb("att", [P, 2, HEADS * D])
                prod = sb("prod", [P, 2, HEADS * D])
                scored = sb("scored", [P, NT, D + HEADS])
                target = sb("target", [P, NT, HEADS])
                att_in = [k.in_[n][layer].rearrange("h (a c) -> a (h c)", a=1)
                          for n in ("L2_gnn_att_src", "L2_gnn_att_dst")]
                load_all(nc, k, [
                    (conv_w[:, :], k.in_["L2_gnn_conv_w"][layer]),
                    (proj_w[:, :], k.in_["L2_gnn_proj_w"][layer]),
                    (skip_w[:, :], k.in_["L2_gnn_skip_w"][layer]),
                    (att[0:1, 0, :], k.in_["L2_gnn_att_src"][layer:layer + 1].rearrange(
                        "a h c -> a (h c)")),
                    (att[0:1, 1, :], k.in_["L2_gnn_att_dst"][layer:layer + 1].rearrange(
                        "a h c -> a (h c)"))] + [
                    (col[:, j:j + 1], k.in_["L2_gnn_" + n][layer].rearrange("(p a) -> p a", a=1))
                    for j, n in enumerate(("conv_b", "proj_b", "skip_b"))])
                with nc.Block() as block:
                    @block.tensor
                    def _(pe):
                        for a in range(2):
                            ins = pe.matmul(k.ps[:, a * 512:(a + 1) * 512], k.ones[0:1, :],
                                            att[0:1, a, :], start=True, stop=True)
                        ins.then_inc(k.pe_done.sem, 1)
                        k.pe_done.advance(1)

                    @block.vector
                    def _(dve):
                        c = Chain(k.dve_step)
                        dve.wait_ge(k.pe_done.sem, k.pe_done.base)
                        for a in range(2):
                            c.then_wait(dve, dve.tensor_tensor(prod[:, a, :],
                                                               k.ps[:, a * 512:(a + 1) * 512],
                                                               conv_w[:, :], ALU.mult))
                        c.then_wait(dve, dve.tensor_reduce(
                            score_w[:, :], prod[:, :, :].rearrange("p a (h c) -> p (a h) c", c=D),
                            AX.X, ALU.add))
                        c.then_wait(dve, dve.tensor_tensor(col[:, 3:4], col[:, 1:2], col[:, 2:3],
                                                           ALU.add))
                with nc.Block() as block:
                    @block.tensor
                    def _(pe):
                        for i in range(NT):
                            ins = pe.matmul(k.ps[:, i * 8:i * 8 + 8], gT[:, i * P:(i + 1) * P],
                                            score_w[:, :], start=True, stop=True)
                        ins.then_inc(k.pe_done.sem, 1)
                        k.pe_done.advance(1)

                    @block.vector
                    def _(dve):
                        c = Chain(k.dve_step)
                        c.then_wait(dve, dve.tensor_copy(scored[:, :, 0:D], own[:, :, :]))
                        dve.wait_ge(k.pe_done.sem, k.pe_done.base)
                        sc = k.ps[:, 0:NT * 8].rearrange("p (i a h) -> p i a h", a=2, h=HEADS)
                        c.then_wait(dve, dve.tensor_copy(scored[:, :, D:D + HEADS], sc[:, :, 0, :]))
                        c.then_wait(dve, dve.tensor_copy(target[:, :, :], sc[:, :, 1, :]))
                load_all(nc, k, [
                    (k.scored_d.rearrange("(i p) f -> p i f", p=P), scored[:, :, :]),
                    (k.target_d.rearrange("(i p) f -> p i f", p=P), target[:, :, :])])
                with nc.Block() as block:
                    @block.gpsimd
                    def _(pool):
                        for i in range(NT):
                            pool.indirect_dma_start(
                                k.start_d, bass.IndirectOffsetOnAxis(ap=k.first_edge[:, i:i + 1],
                                                                     axis=0),
                                target[:, i, :], None).then_inc(k.fetched.sem, 16)
                        k.fetched.advance(16 * NT)
                        pool.wait_ge(k.fetched.sem, k.fetched.base)
            with ExitStack() as ctx:
                asE = ctx.enter_context(nc.sbuf_tensor(f"l2_asE_{layer}", [P, ETP, HEADS], F32))
                fetch_attention(nc, k, asE)
                edge_weights(nc, k, asE, exS, keep, res_f, res_b)
            with ExitStack() as ctx:
                U = ctx.enter_context(nc.sbuf_tensor(f"l2_U_{layer}", [P, WIN_SLIM, UW], F32))
                inv = ctx.enter_context(nc.sbuf_tensor(f"l2_inv_{layer}", [P, WIN_SLIM], F32))
                attend(nc, k, exS, U)
                UT = ctx.enter_context(nc.sbuf_tensor(f"l2_UT_{layer}", [P, HEADS, NPAD], F32))

                def scale(dve):
                    yield dve.tensor_scalar(inv[:, :], U[:, :, D], 1e-16, None, ALU.add)
                    yield dve.reciprocal(inv[:, :], inv[:, :])
                    yield dve.tensor_scalar(inv[:, :], inv[:, :], 1.0 / HEADS, None, ALU.mult)
                    yield dve.tensor_tensor(U[:, :, 0:D], U[:, :, 0:D], bc(inv[:, :], 2, D),
                                            ALU.mult)
                    yield dve.memset(UT[:, :, WIN_SLIM * W_SLIM:NPAD], 0.0)
                vector_ops(nc, k, scale)
                rounds = [list(range(a, min(a + 4, WIN_SLIM))) for a in range(0, WIN_SLIM, 4)]
                with nc.Block() as block:
                    @block.tensor
                    def _(pe):
                        for r, ws in enumerate(rounds):
                            if r >= 8:
                                pe.wait_ge(k.dve_done.sem, k.dve_done.at(r - 7))
                            for x, w in enumerate(ws):
                                c0 = (r % 8) * 512 + x * P
                                ins = pe.transpose(k.ps[:, c0:c0 + P], U[:, w, 0:D],
                                                   k.ident[:, :])
                            ins.then_inc(k.pe_done.sem, 1)

                    @block.vector
                    def _(dve):
                        for r, ws in enumerate(rounds):
                            dve.wait_ge(k.pe_done.sem, k.pe_done.at(r + 1))
                            n = len(ws)
                            c0 = (r % 8) * 512
                            dve.tensor_copy(
                                UT[:, :, r * P:r * P + n * W_SLIM].rearrange(
                                    "f h (w j) -> f h w j", j=W_SLIM),
                                k.ps[:, c0:c0 + n * P].rearrange(
                                    "f (w h j) -> f h w j", h=HEADS, j=W_SLIM)
                            ).then_inc(k.dve_done.sem, 1)
                        dve.wait_ge(k.dve_done.sem, k.dve_done.at(len(rounds)))
                k.pe_done.advance(len(rounds))
                k.dve_done.advance(len(rounds))
                cT = U[:, :, :].rearrange("p w f -> p (w f)")[:, 0:NPAD]
                out_T = U[:, :, :].rearrange("p w f -> p (w f)")[:, NPAD:2 * NPAD]
                pieces = banks(NPAD)
                with nc.Block() as block:
                    @block.tensor
                    def _(pe):
                        for a, m in pieces:
                            for h in range(HEADS):
                                ins = pe.matmul(k.ps[:, a:a + m], conv_w[:, h * D:(h + 1) * D],
                                                UT[:, h, a:a + m], start=(h == 0),
                                                stop=(h == HEADS - 1))
                            ins.then_inc(k.pe_done.sem, 1)
                        for j, (a, m) in enumerate(pieces):
                            pe.wait_ge(k.act_done.sem, k.act_done.at(j + 1))
                            pe.matmul(k.ps[:, a:a + m], proj_w[:, :], cT[:, a:a + m], start=True,
                                      stop=False)
                            pe.matmul(k.ps[:, a:a + m], skip_w[:, :], gT[:, a:a + m], start=False,
                                      stop=True).then_inc(k.pe_done.sem, 1)

                    @block.scalar
                    def _(act):
                        for j, (a, m) in enumerate(pieces):
                            act.wait_ge(k.pe_done.sem, k.pe_done.at(j + 1))
                            act.activation(cT[:, a:a + m], k.ps[:, a:a + m], ACT.Relu,
                                           bias=col[:, 0:1]).then_inc(k.act_done.sem, 1)
                        for j, (a, m) in enumerate(pieces):
                            act.wait_ge(k.pe_done.sem, k.pe_done.at(len(pieces) + j + 1))
                            act.activation(out_T[:, a:a + m], k.ps[:, a:a + m], ACT.Identity,
                                           bias=col[:, 3:4]).then_inc(k.act_done.sem, 1)
                        act.wait_ge(k.act_done.sem, k.act_done.at(2 * len(pieces)))
                k.pe_done.advance(2 * len(pieces))
                k.act_done.advance(2 * len(pieces))
                vector_ops(nc, k, lambda dve: iter([dve.tensor_copy(k.xT[:, :], out_T[:, :])]))
            to_node_major(nc, k, k.xT, gN)
        vector_ops(nc, k, lambda dve: iter([dve.tensor_tensor(
            gN[:, :, :], gN[:, :, :], k.xN[:, :, :], ALU.add)]))
        layernorm(nc, k, gN, k.xN)
    to_feature_major(nc, k, k.xN, k.xT)



def normalise_weights(nc, k):
    ROWS = 125
    with ExitStack() as ctx:
        def sb(name, shape):
            return ctx.enter_context(nc.sbuf_tensor("nw_" + name, shape, F32))
        w = sb("w", [ROWS, E // ROWS])
        mm = sb("mm", [ROWS, 2])
        row = sb("row", [1, 2, ROWS])
        ends = sb("ends", [1, 4])
        both = sb("both", [P, 2])
        load_all(nc, k, [(w[:, :], k.in_["edge_weight"].rearrange("(p t) -> p t", p=ROWS))])

        def ops(dve):
            yield dve.tensor_reduce(mm[:, 0:1], w[:, :], AX.X, ALU.max)
            yield dve.tensor_reduce(mm[:, 1:2], w[:, :], AX.X, ALU.min)
        vector_ops(nc, k, ops)

        def evac(dve):
            yield dve.tensor_copy(row[:, :, :].rearrange("p a r -> p (a r)"), k.ps[0:1, 0:2 * ROWS])
            yield dve.tensor_reduce(ends[:, 0:1], row[:, 0, :], AX.X, ALU.max)
            yield dve.tensor_reduce(ends[:, 1:2], row[:, 1, :], AX.X, ALU.min)
            yield dve.tensor_tensor(ends[:, 2:3], ends[:, 0:1], ends[:, 1:2], ALU.subtract)
            yield dve.tensor_scalar(ends[:, 2:3], ends[:, 2:3], 1e-8, None, ALU.add)
            yield dve.reciprocal(ends[:, 2:3], ends[:, 2:3])
        turn(nc, k, [(0, mm[:, 0:1]), (ROWS, mm[:, 1:2])], evac)
        with nc.Block() as block:
            @block.tensor
            def _(pe):
                pe.matmul(k.ps[:, 0:2], k.ones[0:1, :], ends[:, 1:3], start=True,
                          stop=True).then_inc(k.pe_done.sem, 1)
                k.pe_done.advance(1)

            @block.vector
            def _(dve):
                c = Chain(k.dve_step)
                dve.wait_ge(k.pe_done.sem, k.pe_done.base)
                c.then_wait(dve, dve.tensor_copy(both[:, :], k.ps[:, 0:2]))
                c.then_wait(dve, dve.tensor_scalar(k.weight_step[:, :], k.weight_step[:, :],
                                                   both[:, 0:1], both[:, 1:2], ALU.subtract, ALU.mult))


def layer3(nc, k):
    normalise_weights(nc, k)
    with ExitStack() as ctx:
        def sb(name, shape):
            return ctx.enter_context(nc.sbuf_tensor("l3_" + name, shape, F32))
        w = [sb(f"w{l}", [P, REL, D]) for l in range(2)]
        root = [sb(f"root{l}", [P, D]) for l in range(2)]
        bias = sb("bias", [1, 2, D])
        table = sb("table", [P, RING, REL * D])
        hN = sb("hN", [P, NT, D])
        load_all(nc, k, [x for l in range(2) for x in (
            (w[l][:, :, :], k.in_[f"L3_gnn_W{l + 1}"].rearrange("r i o -> i r o")),
            (root[l][:, :], k.in_[f"L3_gnn_root{l + 1}"]),
            (bias[:, l, :], k.in_[f"L3_gnn_b{l + 1}"].rearrange("(a o) -> a o", a=1)))])
        for l in range(2):
            with nc.Block() as block:
                @block.tensor
                def _(pe):
                    for i in range(NT):
                        if i >= RING:
                            pe.wait_ge(k.dve_done.sem, k.dve_done.at(i - RING + 1))
                        b = (i % RING) * 512
                        pe.matmul(k.ps[:, b:b + 512], k.xT[:, i * P:(i + 1) * P],
                                  w[l][:, :, :].rearrange("i r o -> i (r o)"), start=True,
                                  stop=True).then_inc(k.pe_done.sem, 1)

                @block.vector
                def _(dve):
                    for i in range(NT):
                        dve.wait_ge(k.pe_done.sem, k.pe_done.at(i + 1))
                        if i >= RING:
                            dve.wait_ge(k.row_load[i % RING].sem, k.row_load[i % RING].at(
                                16 * (i // RING)))
                        b = (i % RING) * 512
                        dve.tensor_copy(table[:, i % RING, :], k.ps[:, b:b + 512]).then_inc(
                            k.dve_done.sem, 1)

                @block.sync
                def _(sp):
                    for i in range(NT):
                        sp.wait_ge(k.dve_done.sem, k.dve_done.at(i + 1))
                        sp.dma_start(k.rel_d[i * P:(i + 1) * P, :], table[:, i % RING, :]).then_inc(
                            k.row_load[i % RING].sem, 16)
                    for j in range(RING):
                        k.row_load[j].advance(16 * len(range(j, NT, RING)))
                        sp.wait_ge(k.row_load[j].sem, k.row_load[j].base)
            k.pe_done.advance(NT)
            k.dve_done.advance(NT)
            aggregate(nc, k, k.rel_d.rearrange("n (r o) -> (n r) o", r=REL), k.rel_step, k.weight_step,
                      init_root(k, k.xT, root[l][:, :], bias[:, l, :]))
            if l == 0:
                vector_ops(nc, k, lambda dve: iter([dve.tensor_scalar(
                    hN[:, :, :], acc_view(k), 0.0, None, ALU.max)]))
                to_feature_major(nc, k, hN, k.xT)
            else:
                vector_ops(nc, k, lambda dve: iter([dve.tensor_tensor(
                    hN[:, :, :], acc_view(k), k.xN[:, :, :], ALU.add)]))
        layernorm(nc, k, hN, k.xN)



def build(nc, ins, out, stop=9):
    k = Net()
    k.in_ = ins
    tags = iter(range(1000))
    k.tag = lambda: next(tags)
    with ExitStack() as ctx:
        def sb(name, shape, dt=F32):
            return ctx.enter_context(nc.sbuf_tensor(name, shape, dt))

        def dram(name, shape, dt=F32):
            return nc.dram_tensor(name, shape, dt, kind="Internal").ap()

        def sig(name):
            return Signal(nc, ctx, name)
        k.moved, k.pe_done, k.act_done = sig("moved"), sig("pe_done"), sig("act_done")
        k.dve_done, k.pool_done, k.dve_step = sig("dve_done"), sig("pool_done"), sig("dve_step")
        k.idx_ready, k.tick, k.part, k.added = sig("idx_ready"), sig("tick"), sig("part"), sig("added")
        k.used = [sig(f"used{a}") for a in range(2)]
        k.built = [sig(f"built{a}") for a in range(2)]
        k.spilled = [sig(f"spilled{a}") for a in range(2)]
        k.fetched = sig("fetched")
        k.row_load = [sig(f"row_load{j}") for j in range(RING)]
        k.row_in = [sig(f"row_in{j}") for j in range(RING)]
        k.ps = ctx.enter_context(nc.psum_tensor("ps", [P, 8 * 512], F32))

        k.xN, k.xT = sb("xN", [P, NT, D]), sb("xT", [P, NPAD])
        k.iota_row, k.iota_bf = sb("iota_row", [P, P]), sb("iota_bf", [P, P], BF16)
        k.ident, k.before = sb("ident", [P, P]), sb("before", [P, P])
        k.ones, k.zeros = sb("ones", [P, P]), sb("zeros", [P, P])
        k.part_id, k.step_id = sb("part_id", [P, 1]), sb("step_id", [P, 4])
        k.node_id, k.tile_id = sb("node_id", [P, NT]), sb("tile_id", [1, ETP])
        k.norm = sb("norm", [P, 2, NT])
        k.first_edge = sb("first_edge", [P, NT], I32)
        k.first_dst = sb("first_dst", [RP, CH], I32)
        k.src_tile = sb("src_tile", [P, ETP], I32)
        k.src_step, k.rel_step = sb("src_step", [P, 512], I32), sb("rel_step", [P, 512], I32)
        k.weight_step = sb("weight_step", [P, 512])
        k.local_wide, k.local_slim = sb("local_wide", [P, 512]), sb("local_slim", [P, 512])
        k.tile_slim = sb("tile_slim", [P, 4], I32)
        k.win_wide, k.win_slim = sb("win_wide", [1, 512], I32), sb("win_slim", [1, 512], I32)
        k.tile_slim_row = sb("tile_slim_row", [1, 512], I32)
        k.chain = sb("chain", [HEADS, 3, ETP])

        k.edges_d = dram("edges_d", (ETP, 4 * P))
        k.stepi_d, k.stepf_d = dram("stepi_d", (2, 512), I32), dram("stepf_d", (1, 512))
        k.rows_d = dram("rows_d", (NPAD, D))
        k.scored_d = dram("scored_d", (NPAD, D + HEADS))
        k.target_d = dram("target_d", (NPAD, HEADS))
        k.start_d = dram("start_d", (ETP * P + NPAD, HEADS))
        k.spill_d = dram("spill_d", (ETP * P, D))
        k.exp_d = dram("exp_d", (ETP, HEADS * P))
        k.rel_d = dram("rel_d", (NPAD, REL * D))

        with ExitStack() as early:
            edF = ctx.enter_context(nc.sbuf_tensor("edF", [RP, CH, 4, P], F32))
            k.int_a = early.enter_context(nc.sbuf_tensor("int_a", [P, P], I32))
            k.int_b = early.enter_context(nc.sbuf_tensor("int_b", [P, 32], I32))
            k.int_c = early.enter_context(nc.sbuf_tensor("int_c", [P, ETP], I32))
            k.win_f_row = early.enter_context(nc.sbuf_tensor("win_f_row", [1, 512], F32))
            tile_wide = early.enter_context(nc.sbuf_tensor("tile_wide", [P, 4], I32))
            dstE = early.enter_context(nc.sbuf_tensor("dstE", [P, ETP], F32))
            srcE = early.enter_context(nc.sbuf_tensor("srcE", [P, ETP], F32))
            constants(nc, k)
            edge_rows(nc, k, edF)
            edge_columns(nc, k, edF, dstE, srcE)
            vector_ops(nc, k, lambda dve: iter([dve.tensor_scalar(
                k.first_dst[:, :], edF[:, :, 0, 0], float(N - 1), None, ALU.min)]))
            degrees(nc, k, dstE, srcE)
            staircase(nc, k, W_WIDE, 7, tile_wide, k.win_wide, D, None)
            step_edges(nc, k, W_WIDE, tile_wide, k.local_wide, True)
            staircase(nc, k, W_SLIM, 5, k.tile_slim, k.win_slim, UW, k.tile_slim_row)
            step_edges(nc, k, W_SLIM, k.tile_slim, k.local_slim, False)
        layer0(nc, k)
        if stop > 1:
            layer1(nc, k)
        if stop > 2:
            layer2(nc, k, edF)
        if stop > 3:
            layer3(nc, k)
        top = (NT - 1) * P
        load_all(nc, k, [(out[0:top, :].rearrange("(i p) f -> p i f", p=P), k.xN[:, 0:NT - 1, :]),
                         (out[top:N, :], k.xN[0:LASTN, NT - 1, :])])


NAMES = ["x", "src", "dst", "edge_type_4", "edge_weight",
         "L1_gnn_W_mlp", "L1_gnn_b_mlp", "L1_gnn_gamma1", "L1_gnn_beta1", "L1_gnn_W_conv",
         "L1_gnn_b_conv", "L1_gnn_gamma2", "L1_gnn_beta2",
         "L2_gnn_conv_w", "L2_gnn_att_src", "L2_gnn_att_dst", "L2_gnn_conv_b", "L2_gnn_proj_w",
         "L2_gnn_proj_b", "L2_gnn_skip_w", "L2_gnn_skip_b",
         "L3_gnn_W1", "L3_gnn_root1", "L3_gnn_b1", "L3_gnn_W2", "L3_gnn_root2", "L3_gnn_b2"]


def kernel(**inputs):
    import concourse.bacc as bacc
    from concourse.bass_utils import run_bass_kernel_spmd as run

    nc = bacc.Bacc("TRN2", target_bir_lowering=False, num_devices=1)
    arrays, args = {}, {}
    for name in NAMES:
        a = np.ascontiguousarray(inputs[name])
        arrays["in_" + name] = a
        args[name] = nc.dram_tensor("in_" + name, a.shape, mybir.dt.from_np(a.dtype),
                                    kind="ExternalInput").ap()
    out = nc.dram_tensor("out", (N, D), F32, kind="ExternalOutput").ap()
    build(nc, args, out)
    r = run(nc, [arrays], core_ids=[0])
    return r.results[0]["out"]
```
